# Optimizing a Trainium2 kernel written in Bass

```python
import numpy as np
import jax
import jax.numpy as jnp

def _softmax(x, axis=-1):
    return jax.nn.softmax(x, axis=axis)

def _gelu(x):
    return jax.nn.gelu(x, approximate=True)

def _silu(x):
    return jax.nn.silu(x)

def _sigmoid(x):
    return jax.nn.sigmoid(x)

def _layernorm(x, axis=-1, eps=1e-05):
    m = jnp.mean(x, axis=axis, keepdims=True)
    v = jnp.var(x, axis=axis, keepdims=True)
    return (x - m) / jnp.sqrt(v + eps)

def _scatter_add(tgt, idx, src, axis=0):
    return tgt.at[idx].add(src)

def _segment_sum(src, seg, n):
    return jax.ops.segment_sum(src, seg, n)
kernel_name = 'mk_adj_resnorm_d1_adj_r2_861bd2'

def setup_inputs(seed: int=0):
    np.random.seed(seed)
    _w = jnp.asarray

    def _rec_inputs():
        import jax
        import jax.numpy as jnp
        _gk = jax.random.key(seed)
        x = -0.0001538 + 1 * jax.random.normal(jax.random.fold_in(_gk, 1), (64, 128, 384), jnp.float32)
        _a = jax.random.bernoulli(jax.random.fold_in(_gk, 2), 0.015625, (64, 128, 128))
        _a = jnp.logical_or(_a, jnp.swapaxes(_a, -1, -2))
        _a = jnp.logical_or(_a, jnp.eye(128, dtype=bool))
        _af = _a.astype(jnp.float32)
        _af = _af * jax.random.uniform(jax.random.fold_in(_gk, 3), (64, 128, 128), jnp.float32, 0.05, 4.42607)
        adj = _af
        return (x, adj)
    x, adj = _rec_inputs()

    def _L0_gnn_setup():
        import jax, jax.numpy as jnp
        import numpy as np
        NUM_HEADS = 12
        HIDDEN = 384
        HEAD = HIDDEN // NUM_HEADS
        B, N = (16, 256)
        key = jax.random.key(seed)
        ks = jax.random.split(key, 9)
        s = 0.02
        return {'x': jax.random.normal(ks[0], (B, N, HIDDEN), jnp.float32), 'spatial_encoding': jax.random.normal(ks[1], (B, N, N), jnp.float32), 'edge_encoding': jax.random.normal(ks[2], (B, N, N), jnp.float32), 'Wq': jax.random.normal(ks[3], (HIDDEN, HIDDEN), jnp.float32) * s, 'Wk': jax.random.normal(ks[4], (HIDDEN, HIDDEN), jnp.float32) * s, 'Wv': jax.random.normal(ks[5], (HIDDEN, HIDDEN), jnp.float32) * s, 'bv': jax.random.normal(ks[6], (HIDDEN,), jnp.float32) * s, 'Wo': jax.random.normal(ks[7], (HIDDEN, HIDDEN), jnp.float32) * s, 'bo': jax.random.normal(ks[8], (HIDDEN,), jnp.float32) * s}
    _L0_gnn_all = _L0_gnn_setup()
    _L0_gnn_in = {k: v for k, v in _L0_gnn_all.items() if k in ('Wq', 'Wk', 'Wv', 'bv', 'Wo', 'bo')}
    del _L0_gnn_all
    return {'x': x, 'adj': adj, 'L0_gnn_Wq': _L0_gnn_in['Wq'], 'L0_gnn_Wk': _L0_gnn_in['Wk'], 'L0_gnn_Wv': _L0_gnn_in['Wv'], 'L0_gnn_bv': _L0_gnn_in['bv'], 'L0_gnn_Wo': _L0_gnn_in['Wo'], 'L0_gnn_bo': _L0_gnn_in['bo']}

def reference(x, adj, L0_gnn_Wq, L0_gnn_Wk, L0_gnn_Wv, L0_gnn_bv, L0_gnn_Wo, L0_gnn_bo):
    import jax
    import jax.numpy as jnp

    def _L0_gnn_ref(x, spatial_encoding, edge_encoding, Wq, Wk, Wv, bv, Wo, bo):
        import jax, jax.numpy as jnp
        import numpy as np
        NUM_HEADS = 12
        HIDDEN = 384
        HEAD = HIDDEN // NUM_HEADS
        B, N = (16, 256)
        b, n, h = x.shape
        scale = jnp.asarray(HIDDEN, x.dtype) ** (-0.5)
        q = (x @ Wq.T).reshape(b, n, NUM_HEADS, HEAD)
        k = (x @ Wk.T).reshape(b, n, NUM_HEADS, HEAD)
        v = (x @ Wv.T + bv).reshape(b, n, NUM_HEADS, HEAD)
        bias = (spatial_encoding + edge_encoding)[:, None]
        scores = jnp.einsum('bqhd,bkhd->bhqk', q, k) * scale + bias
        row_nonzero = jnp.any(scores != 0, axis=-1, keepdims=True)
        scores = jnp.where(row_nonzero, scores, -jnp.inf)
        p = jax.nn.softmax(scores, axis=-1)
        p = jnp.nan_to_num(p)
        out = jnp.einsum('bhqk,bkhd->bqhd', p, v).reshape(b, n, h)
        return out @ Wo.T + bo
    x = _layernorm(x + _L0_gnn_ref(x, adj, adj, L0_gnn_Wq, L0_gnn_Wk, L0_gnn_Wv, L0_gnn_bv, L0_gnn_Wo, L0_gnn_bo), axis=-1)
    return x

_drawn_inputs = setup_inputs


def setup_inputs(seed=0):
    import zlib

    import numpy as np

    out = dict(_drawn_inputs(seed))
    spreads = {}
    factors = {'L0_gnn_Wq': 8.0, 'L0_gnn_Wk': 8.0, 'L0_gnn_bv': 6.292, 'L0_gnn_bo': 2.988}
    for name, (base, spread) in spreads.items():
        noise = np.random.default_rng([zlib.crc32(name.encode()), seed]).standard_normal(out[name].shape)
        drawn = base * np.exp(spread * noise) if base else spread * noise
        out[name] = jnp.asarray(drawn.astype(out[name].dtype))
    for name, factor in factors.items():
        out[name] = (out[name] * factor).astype(out[name].dtype)
    return out
```

```python
from contextlib import ExitStack

import concourse.bass as bass
from concourse import mybir

FP32 = mybir.dt.float32
FP32R = mybir.dt.float32r
ALU = mybir.AluOpType
ACT = mybir.ActivationFunctionType
AX = mybir.AxisListType


def graph_attention_layernorm(nc, x, adj, wq, wk, wv, bv, wo, bo, out):
    GRAPHS, N, C = x.shape
    HEADS = 12
    D = C // HEADS
    P = 128
    CK = C // P
    QUAD = 4
    TOK = QUAD * N
    QUADS = GRAPHS // QUAD
    PAIRS = QUADS // 2
    RG = P // D
    HB = HEADS // RG
    DV = D + 1
    SCALE = float(C) ** -0.5
    EPS = 1e-5
    NEG_INIT = 3.0e38

    x_quads = x.rearrange("(q g) p c -> q p g c", g=QUAD)
    adj_quads = adj.rearrange("(q g) p k -> q p g k", g=QUAD)

    STAGES = [("x", 0), ("x", 1), ("x", 2), ("q", 0), ("k", 0), ("v", 0), ("q", 1), ("k", 1), ("v", 1),
              ("q", 2), ("k", 2), ("v", 2), ("v", 3)]
    FILL = [[[0, 1], [2], [3], [4]], [[5], [], [6], [7]], [[8], [], [9], [10]], [[], [], [11], [12]]]
    NS = len(STAGES)
    W_USES = 4 * CK

    with ExitStack() as ctx:
        def sb(name, shape, dt=FP32):
            return ctx.enter_context(nc.sbuf_tensor(name, shape, dt))

        def ps(name):
            return ctx.enter_context(nc.psum_tensor(name, [P, 512], FP32))

        def sem(name):
            return ctx.enter_context(nc.semaphore(name))

        ident = sb("ident", [P, P])
        w_nat = sb("w_nat", [P, 4, CK, C])
        w_hi = sb("w_hi", [P, 4, CK, C], FP32R)
        w_lo = sb("w_lo", [P, 4, CK, C], FP32R)
        bv_row = sb("bv_row", [P, C])
        bo_row = sb("bo_row", [P, C])
        x_sb = [sb(f"x_sb{n}", [P, QUAD, C]) for n in range(2)]
        adj_sb = [sb(f"adj_sb{n}", [P, QUAD, N]) for n in range(2)]
        adj2 = [sb(f"adj2_{n}", [P, QUAD, N]) for n in range(2)]
        xb = [sb(f"xb{n}", [P, QUAD, C]) for n in range(2)]
        xT_hi = sb("xT_hi", [P, CK, TOK], FP32R)
        xT_lo = sb("xT_lo", [P, CK, TOK], FP32R)
        qT = [sb(f"qT{n}", [P, CK, TOK]) for n in range(2)]
        kT = [sb(f"kT{n}", [P, CK, TOK]) for n in range(2)]
        v_sb = [sb(f"v_sb{n}", [P, QUAD, HEADS, DV]) for n in range(2)]
        neg_scores = [sb(f"neg_scores{n}", [P, HEADS, N]) for n in range(2)]
        probs = [sb(f"probs{n}", [P, HEADS, N]) for n in range(2)]
        probsT = [sb(f"probsT{n}", [P, HB, N]) for n in range(2)]
        neg_max = [sb(f"neg_max{n}", [P, HEADS]) for n in range(2)]
        neg_min = sb("neg_min", [P, HEADS])
        extent = [sb(f"extent{n}", [P, HEADS]) for n in range(2)]
        recip = sb("recip", [P, HEADS])
        weight = sb("weight", [P, HEADS])
        o_sb = sb("o_sb", [P, C])
        oT_hi = sb("oT_hi", [P, CK, N], FP32R)
        oT_lo = sb("oT_lo", [P, CK, N], FP32R)
        z_sb = [sb(f"z_sb{n}", [P, C]) for n in range(2)]
        bn = sb("bn", [P, 6])
        mean_var = [sb(f"mean_var{n}", [P, 2]) for n in range(2)]
        minus_half = sb("minus_half", [P, 1])
        var_eps = sb("var_eps", [P, 1])
        rstd = sb("rstd", [P, 1])
        shift = sb("shift", [P, 1])
        y_out = [sb(f"y_out{n}", [P, C]) for n in range(2)]

        ps_scores = [ps(f"ps_scores{n}") for n in range(2)]
        ps_probsT = [ps(f"ps_probsT{n}") for n in range(2)]
        ps_proj = [ps(f"ps_proj{n}") for n in range(2)]
        ps_o = ps("ps_o")
        ps_y = ps("ps_y")

        w_loaded = [sem(f"w_loaded{n}") for n in range(4)]
        b_loaded = sem("b_loaded")
        x_loaded = [sem(f"x_loaded{n}") for n in range(2)]
        adj_loaded = [sem(f"adj_loaded{n}") for n in range(2)]
        stored = [sem(f"stored{n}") for n in range(2)]
        consts_set = sem("consts_set")
        w_turned = sem("w_turned")
        w_high = sem("w_high")
        w_split = sem("w_split")
        x_turned = sem("x_turned")
        x_high = sem("x_high")
        x_split = sem("x_split")
        qk_ready = sem("qk_ready")
        qk_done = sem("qk_done")
        v_ready = sem("v_ready")
        v_done = sem("v_done")
        adj_doubled = sem("adj_doubled")
        xb_done = sem("xb_done")
        scores_ready = sem("scores_ready")
        biased = sem("biased")
        probs_done = sem("probs_done")
        p_turned = sem("p_turned")
        pT_done = sem("pT_done")
        o_ready = sem("o_ready")
        min_done = sem("min_done")
        extent_done = sem("extent_done")
        recip_done = sem("recip_done")
        weight_done = sem("weight_done")
        o_done = sem("o_done")
        o_turned = sem("o_turned")
        o_high = sem("o_high")
        o_split = sem("o_split")
        y_ready = sem("y_ready")
        z_done = sem("z_done")
        bn_done = sem("bn_done")
        stats_done = sem("stats_done")
        eps_done = sem("eps_done")
        rstd_done = sem("rstd_done")
        shift_done = sem("shift_done")
        passed = sem("passed")
        normed = sem("normed")

        block = ctx.enter_context(nc.Block())

        def wait(eng, s, n):
            if not isinstance(n, int) or n > 0:
                eng.wait_ge(s, n)

        def stand(eng):
            eng.sem_inc(passed, 1)

        def stage_done(k, q):
            if k < 0:
                k, q = k + NS, q - 1
            kind, c = STAGES[k]
            if kind == "x":
                return x_split, 3 * q + c + 1
            if kind == "v":
                return v_done, QUAD * q + c + 1
            return qk_done, 6 * q + 2 * c + (2 if kind == "k" else 1)

        def bank_of(k, parity):
            return ps_proj[(W_USES + NS * parity + k) % 2]

        def run(eng, slot, tail):
            def pair(i, first, last):
                for parity in range(2):
                    q = 2 * i + parity
                    for g in range(QUAD):
                        j = parity * QUAD + g
                        slot(2 * QUAD * i + j, g, q, parity, True, not first or j >= 1, not first or j >= 2,
                             not last or parity == 0, not last)

            pair(0, True, False)
            with eng.Fori(1, PAIRS - 1) as i:
                pair(i, False, False)
            pair(PAIRS - 1, False, True)
            if tail:
                slot(GRAPHS, 0, QUADS, 0, False, True, True, False, False)
                slot(GRAPHS + 1, 1, QUADS, 0, False, False, True, False, False)

        @block.sync
        def _(sp):
            def load(q, parity):
                sp.dma_start(x_sb[parity][:, :, :], x_quads[q]).then_inc(x_loaded[parity], 16)
                sp.dma_start(adj_sb[parity][:, :, :], adj_quads[q]).then_inc(adj_loaded[parity], 16)

            load(0, 0)
            for n, w in enumerate((wq, wk, wv, wo)):
                sp.dma_start(w_nat[:, n, :, :], w.rearrange("(t p) c -> p t c", p=P)).then_inc(w_loaded[n], 16)
            for row, b in ((bv_row, bv), (bo_row, bo)):
                sp.dma_start(row[:, :], b.rearrange("(a c) -> a c", a=1).to_broadcast([P, C])).then_inc(b_loaded, 16)
            load(1, 1)

            def slot(G, g, Q, parity, new, old, older, ahead, ahead2):
                if g == 0 and ahead2:
                    wait(sp, x_turned, CK * (Q + 1))
                    stand(sp)
                    wait(sp, xb_done, QUAD * (Q + 1))
                    stand(sp)
                    wait(sp, adj_doubled, Q + 1)
                    stand(sp)
                    load(Q + 2, parity)
                if older:
                    wait(sp, normed, G - 1)
                    stand(sp)
                    sp.dma_start(out[G - 2], y_out[g % 2][:, :]).then_inc(stored[g % 2], 16)

            run(sp, slot, True)
            for n in range(2):
                sp.wait_ge(stored[n], 16 * GRAPHS // 2)

        @block.gpsimd
        def _(pool):
            pool.memset(ident[:, :], 0.0).then_inc(consts_set, 1)
            pool.wait_ge(consts_set, 1)
            pool.affine_select(out=ident[:, :], in_=ident[:, :], compare_op=ALU.not_equal, fill=1.0, base=0,
                               pattern=[[-1, P]], channel_multiplier=1).then_inc(consts_set, 1)
            pool.memset(minus_half[:, :], -0.5).then_inc(consts_set, 1)
            for n in range(2):
                pool.memset(v_sb[n][:, :, :, D:DV], 1.0).then_inc(consts_set, 1)
            pool.wait_ge(consts_set, 5)
            pool.wait_ge(b_loaded, 32)

            def double_adj(q, parity, loads):
                wait(pool, adj_loaded[parity], 16 * loads)
                wait(pool, biased, RG * QUAD * (q - 1))
                pool.tensor_tensor(adj2[parity][:, :, :], adj_sb[parity][:, :, :], adj_sb[parity][:, :, :],
                                   ALU.add).then_inc(adj_doubled, 1)

            def add_bo(G, g, parity, loads):
                wait(pool, x_loaded[parity], 16 * loads)
                wait(pool, z_done, G - 2 * QUAD + 1)
                pool.tensor_tensor(xb[parity][:, g, :], x_sb[parity][:, g, :], bo_row[:, :],
                                   ALU.add).then_inc(xb_done, 1)

            double_adj(0, 0, 1)
            for g in range(QUAD):
                add_bo(g, g, 0, 1)

            def normalise(G, n, stores):
                wait(pool, stats_done, G + 1)
                stand(pool)
                pool.tensor_scalar(var_eps[:, :], mean_var[n][:, 1:2], 1.0, EPS, ALU.mult, ALU.add)\
                    .then_inc(eps_done, 1)
                wait(pool, eps_done, G + 1)
                pool.tensor_tensor(rstd[:, :], var_eps[:, :], minus_half[:, :], ALU.pow).then_inc(rstd_done, 1)
                wait(pool, rstd_done, G + 1)
                stand(pool)
                pool.tensor_scalar(shift[:, :], mean_var[n][:, 0:1], -1.0, rstd[:, 0:1], ALU.mult, ALU.mult)\
                    .then_inc(shift_done, 1)
                wait(pool, shift_done, G + 1)
                wait(pool, stored[n], 16 * stores)
                stand(pool)
                pool.tensor_scalar(y_out[n][:, :], z_sb[n][:, :], rstd[:, 0:1], shift[:, 0:1], ALU.mult, ALU.add)\
                    .then_inc(normed, 1)

            def slot(G, g, Q, parity, new, old, older, ahead, ahead2):
                nxt = 1 - parity
                if ahead:
                    loads = (Q - parity) // 2 + parity + 1
                    if g == 0:
                        double_adj(Q + 1, nxt, loads)
                    add_bo(G + QUAD, g, nxt, loads)
                if older:
                    normalise(G - 2, g % 2, stores_before(G, parity, g))

            def stores_before(G, parity, g):
                return (G - 2 - g % 2) // 2

            run(pool, slot, True)

        @block.tensor
        def _(pe):
            pe.wait_ge(consts_set, 5)
            use = 0
            for n in range(4):
                pe.wait_ge(w_loaded[n], 16)
                for c in range(CK):
                    if use >= 2:
                        pe.wait_ge(w_split, use - 1)
                    for t in range(CK):
                        mm = pe.transpose(ps_proj[use % 2][:, t * P:(t + 1) * P], w_nat[:, n, t, c * P:(c + 1) * P],
                                          ident[:, :])
                    mm.then_inc(w_turned, 1)
                    use += 1

            def three_pass(dst, lhs_hi, lhs_lo, rhs_hi, rhs_lo):
                for c in range(CK):
                    pe.matmul(dst, lhs_hi(c), rhs_hi(c), start=(c == 0), stop=False)
                    pe.matmul(dst, lhs_lo(c), rhs_hi(c), start=False, stop=False)
                    mm = pe.matmul(dst, lhs_hi(c), rhs_lo(c), start=False, stop=(c == CK - 1))
                return mm

            def stage(k, q, parity, loads):
                kind, c = STAGES[k]
                bank = bank_of(k, parity)
                if isinstance(q, int) and q == 0 and k < 2:
                    wait(pe, w_split, W_USES - 1 + k)
                else:
                    wait(pe, *stage_done(k - 2, q))
                if kind == "x":
                    if c == 0:
                        wait(pe, x_loaded[parity], 16 * loads)
                    for g in range(QUAD):
                        mm = pe.transpose(bank[:, g * N:(g + 1) * N], x_sb[parity][:, g, c * P:(c + 1) * P],
                                          ident[:, :])
                    mm.then_inc(x_turned, 1)
                elif kind == "v":
                    if c == 0:
                        wait(pe, x_split, CK * (q + 1))
                    tok = slice(c * N, (c + 1) * N)
                    three_pass(bank[:, 0:C], lambda i: xT_hi[:, i, tok], lambda i: xT_lo[:, i, tok],
                               lambda i: w_hi[:, 2, i, :], lambda i: w_lo[:, 2, i, :]).then_inc(v_ready, 1)
                else:
                    n = 0 if kind == "q" else 1
                    col = slice(c * P, (c + 1) * P)
                    if isinstance(q, int) and q == 0:
                        wait(pe, w_split, W_USES)
                    wait(pe, x_split, CK * (q + 1))
                    three_pass(bank[:, :], lambda i: w_hi[:, n, i, col], lambda i: w_lo[:, n, i, col],
                               lambda i: xT_hi[:, i, :], lambda i: xT_lo[:, i, :]).then_inc(qk_ready, 1)

            def scores(G, g, Q, parity, b):
                if g == 0 and b == 0:
                    wait(pe, qk_done, 6 * (Q + 1))
                wait(pe, biased, RG * G + b - 1)
                tok = slice(g * N, (g + 1) * N)
                rows = slice(b * D, (b + 1) * D)
                for i in range(HB):
                    mm = pe.matmul(ps_scores[b % 2][:, i * N:(i + 1) * N], qT[parity][rows, i, tok],
                                   kT[parity][rows, i, tok], start=True, stop=True)
                mm.then_inc(scores_ready, 1)

            def turn_probs(G, n, b):
                wait(pe, probs_done, RG * G + b + 1)
                wait(pe, pT_done, RG * G + b - 1)
                for i in range(HB):
                    mm = pe.transpose(ps_probsT[b % 2][:, i * N:(i + 1) * N], probs[n][:, b * HB + i, :], ident[:, :])
                mm.then_inc(p_turned, 1)

            def probs_times_v(G, g, parity, b):
                if b == 0:
                    wait(pe, v_done, G + 1)
                    wait(pe, o_done, G)
                wait(pe, pT_done, RG * G + b + 1)
                for i in range(HB):
                    h = b + RG * i
                    mm = pe.matmul(ps_o[:, h * DV:(h + 1) * DV], probsT[b % 2][:, i, :], v_sb[parity][:, g, h, :],
                                   start=True, stop=True)
                if b == RG - 1:
                    mm.then_inc(o_ready, 1)

            def turn_heads(G):
                wait(pe, o_done, G + 1)
                wait(pe, z_done, G)
                for c in range(CK):
                    mm = pe.transpose(ps_y[:, c * N:(c + 1) * N], o_sb[:, c * P:(c + 1) * P], ident[:, :])
                mm.then_inc(o_turned, 1)

            def project_out(G):
                wait(pe, o_split, G + 1)
                three_pass(ps_y[:, 0:C], lambda i: oT_hi[:, i, :], lambda i: oT_lo[:, i, :],
                           lambda i: w_hi[:, 3, i, :], lambda i: w_lo[:, 3, i, :]).then_inc(y_ready, 1)

            for k in range(NS):
                stage(k, 0, 0, 1)

            def slot(G, g, Q, parity, new, old, older, ahead, ahead2):
                was = (g - 1) % QUAD
                was_parity = parity if g else 1 - parity
                for b in range(RG):
                    if new:
                        scores(G, g, Q, parity, b)
                    if old:
                        turn_probs(G - 1, (g - 1) % 2, b)
                    if older and b == 0:
                        turn_heads(G - 2)
                    if older and b == 1:
                        project_out(G - 2)
                    if ahead:
                        for k in FILL[g][b]:
                            stage(k, Q + 1, 1 - parity, (Q - parity) // 2 + parity + 1 if k == 0 else None)
                    if old:
                        probs_times_v(G - 1, was, was_parity, b)

            run(pe, slot, True)

        @block.scalar
        def _(act):
            use = 0
            for n in range(4):
                for c in range(CK):
                    act.wait_ge(w_turned, use + 1)
                    act.activation(w_hi[:, n, c, :], ps_proj[use % 2][:, 0:C], ACT.Copy).then_inc(w_high, 1)
                    use += 1

            def stage(k, q, parity):
                kind, c = STAGES[k]
                bank = bank_of(k, parity)
                if kind == "x":
                    wait(act, x_turned, CK * q + c + 1)
                    act.activation(xT_hi[:, c, :], bank[:, :], ACT.Copy).then_inc(x_high, 1)
                elif kind in ("q", "k"):
                    wait(act, qk_ready, 6 * q + 2 * c + (2 if kind == "k" else 1))
                    dst = (qT if kind == "q" else kT)[parity]
                    act.activation(dst[:, c, :], bank[:, :], ACT.Copy, scale=SCALE if kind == "q" else 1.0)\
                        .then_inc(qk_done, 1)

            for k in range(NS):
                stage(k, 0, 0)

            def slot(G, g, Q, parity, new, old, older, ahead, ahead2):
                for b in range(RG):
                    if old:
                        wait(act, p_turned, RG * (G - 1) + b + 1)
                        act.activation(probsT[b % 2][:, :, :].rearrange("p i n -> p (i n)"),
                                       ps_probsT[b % 2][:, 0:HB * N], ACT.Copy).then_inc(pT_done, 1)
                    if new:
                        wait(act, biased, RG * G + b + 1)
                        for i in range(HB):
                            s = b * HB + i
                            ex = act.activation(probs[g % 2][:, s, :], neg_scores[g % 2][:, s, :], ACT.Exp,
                                                bias=neg_max[g % 2][:, s:s + 1], scale=-1.0)
                        ex.then_inc(probs_done, 1)
                    if older and b == 0:
                        wait(act, o_turned, G - 1)
                        act.activation(oT_hi[:, :, :].rearrange("p c n -> p (c n)"), ps_y[:, 0:C], ACT.Copy)\
                            .then_inc(o_high, 1)
                    if ahead:
                        for k in FILL[g][b]:
                            stage(k, Q + 1, 1 - parity)

            run(act, slot, True)

        @block.vector
        def _(dve):
            use = 0
            for n in range(4):
                for c in range(CK):
                    dve.wait_ge(w_high, use + 1)
                    dve.tensor_tensor(w_lo[:, n, c, :], ps_proj[use % 2][:, 0:C], w_hi[:, n, c, :].bitcast(FP32),
                                      ALU.subtract).then_inc(w_split, 1)
                    use += 1
            dve.wait_ge(b_loaded, 32)

            def stage(k, q, parity):
                kind, c = STAGES[k]
                bank = bank_of(k, parity)
                if kind == "x":
                    wait(dve, x_high, CK * q + c + 1)
                    dve.tensor_tensor(xT_lo[:, c, :], bank[:, :], xT_hi[:, c, :].bitcast(FP32), ALU.subtract)\
                        .then_inc(x_split, 1)
                elif kind == "v":
                    wait(dve, v_ready, QUAD * q + c + 1)
                    dve.tensor_tensor(v_sb[parity][:, c, :, 0:D], bank[:, 0:C].rearrange("p (h d) -> p h d", d=D),
                                      bv_row[:, :].rearrange("p (h d) -> p h d", d=D), ALU.add).then_inc(v_done, 1)

            dve.wait_ge(consts_set, 5)
            for k in range(NS):
                stage(k, 0, 0)

            def add_bias(G, g, Q, parity, b):
                if g == 0 and b == 0:
                    wait(dve, adj_doubled, Q + 1)
                if b == 0:
                    wait(dve, probs_done, RG * (G - 1))
                wait(dve, scores_ready, RG * G + b + 1)
                stand(dve)
                for i in range(HB):
                    s = b * HB + i
                    op = dve.tensor_tensor_reduce(neg_scores[g % 2][:, s, :], ps_scores[b % 2][:, i * N:(i + 1) * N],
                                                  adj2[parity][:, g, :], -1.0, NEG_INIT, ALU.add, ALU.min,
                                                  neg_max[g % 2][:, s:s + 1])
                op.then_inc(biased, 1)

            def find_zero_rows(G, n):
                wait(dve, biased, RG * (G + 1))
                dve.tensor_reduce(neg_min[:, :], neg_scores[n][:, :, :], AX.X, ALU.max).then_inc(min_done, 1)
                wait(dve, min_done, G + 1)
                dve.scalar_tensor_tensor(extent[n][:, :], neg_max[n][:, :], -1.0, neg_min[:, :], ALU.mult, ALU.max)\
                    .then_inc(extent_done, 1)

            def normalise_heads(G, n):
                wait(dve, o_ready, G + 1)
                o_view = ps_o[:, 0:HEADS * DV].rearrange("p (h e) -> p h e", e=DV)
                dve.reciprocal(recip[:, :], o_view[:, :, D]).then_inc(recip_done, 1)
                wait(dve, recip_done, G + 1)
                wait(dve, extent_done, G + 1)
                dve.scalar_tensor_tensor(weight[:, :].rearrange("p (i b) -> p i b", b=RG),
                                         extent[n][:, :].rearrange("p (b i) -> p i b", i=HB), 0.0,
                                         recip[:, :].rearrange("p (i b) -> p i b", b=RG), ALU.not_equal, ALU.mult)\
                    .then_inc(weight_done, 1)
                wait(dve, weight_done, G + 1)
                wait(dve, o_turned, G)
                dve.tensor_tensor(o_sb[:, :].rearrange("p (h d) -> p h d", d=D), o_view[:, :, 0:D],
                                  weight[:, :].rearrange("p (h a) -> p h a", a=1).to_broadcast([P, HEADS, D]),
                                  ALU.mult).then_inc(o_done, 1)

            def split_heads(G):
                wait(dve, o_high, G + 1)
                dve.tensor_tensor(oT_lo[:, :, :].rearrange("p c n -> p (c n)"), ps_y[:, 0:C],
                                  oT_hi[:, :, :].rearrange("p c n -> p (c n)").bitcast(FP32),
                                  ALU.subtract).then_inc(o_split, 1)

            def residual(G, g, parity, n):
                wait(dve, y_ready, G + 1)
                wait(dve, xb_done, G + 1)
                wait(dve, normed, G - 1)
                dve.tensor_tensor(z_sb[n][:, :], ps_y[:, 0:C], xb[parity][:, g, :], ALU.add).then_inc(z_done, 1)
                wait(dve, z_done, G + 1)
                dve.bn_stats(bn[:, :], z_sb[n][:, :]).then_inc(bn_done, 1)
                wait(dve, bn_done, G + 1)
                stand(dve)
                dve.bn_aggr(mean_var[n][:, :], bn[:, :]).then_inc(stats_done, 1)

            def slot(G, g, Q, parity, new, old, older, ahead, ahead2):
                for b in range(RG):
                    if new:
                        add_bias(G, g, Q, parity, b)
                    if older and b == 0:
                        split_heads(G - 2)
                    if ahead:
                        for k in FILL[g][b]:
                            stage(k, Q + 1, 1 - parity)
                    if older and b == 1:
                        residual(G - 2, (g - 2) % QUAD, parity if g >= 2 else 1 - parity, g % 2)
                    if old and b == 2:
                        find_zero_rows(G - 1, (g - 1) % 2)
                if old:
                    normalise_heads(G - 1, (g - 1) % 2)

            run(dve, slot, True)


_INS = ["x", "adj", "L0_gnn_Wq", "L0_gnn_Wk", "L0_gnn_Wv", "L0_gnn_bv", "L0_gnn_Wo", "L0_gnn_bo"]
_OUTS = [((64, 128, 384), "float32")]


def kernel(**inputs):
    import numpy as _np
    import concourse.bacc as _bacc
    from concourse import mybir as _mybir
    from concourse.bass_utils import run_bass_kernel_spmd as _run

    nc = _bacc.Bacc("TRN2", target_bir_lowering=False, num_devices=1)
    arrays, args = {}, []
    for name in _INS:
        a = _np.ascontiguousarray(inputs[name])
        arrays[f"in_{name}_dram"] = a
        args.append(nc.dram_tensor(f"in_{name}_dram", a.shape, _mybir.dt.from_np(a.dtype), kind="ExternalInput").ap())
    for i, (shape, dtype) in enumerate(_OUTS):
        dt = _mybir.dt.from_np(_np.dtype(dtype))
        args.append(nc.dram_tensor(f"out_{i}_dram", shape, dt, kind="ExternalOutput").ap())
    graph_attention_layernorm(nc, *args)
    r = _run(nc, [arrays], core_ids=[0])
    return r.results[0]["out_0_dram"]
```

```python
from contextlib import ExitStack

import concourse.bass as bass
from concourse import mybir

FP32 = mybir.dt.float32
FP32R = mybir.dt.float32r
ALU = mybir.AluOpType
ACT = mybir.ActivationFunctionType
AX = mybir.AxisListType


def graph_attention_layernorm(nc, x, adj, wq, wk, wv, bv, wo, bo, out):
    GRAPHS, N, C = x.shape
    HEADS = 12
    D = C // HEADS
    P = 128
    CK = C // P
    QUAD = 4
    TOK = QUAD * N
    QUADS = GRAPHS // QUAD
    PAIRS = QUADS // 2
    RG = P // D
    HB = HEADS // RG
    DV = D + 1
    SCALE = float(C) ** -0.5
    EPS = 1e-5
    NEG_INIT = 3.0e38

    x_quads = x.rearrange("(q g) p c -> q p g c", g=QUAD)
    adj_quads = adj.rearrange("(q g) p k -> q p g k", g=QUAD)

    STAGES = [("x", 0), ("x", 1), ("x", 2), ("q", 0), ("k", 0), ("q", 1), ("k", 1), ("q", 2), ("k", 2),
              ("v", 0), ("v", 1), ("v", 2), ("v", 3)]
    FILL = [[[0, 1, "turn"], [2], ["out"], [3]], [[4], ["turn", 5], ["out"], [6]],
            [[7], ["turn", 8], ["out"], [9]], [[10], ["turn", 11], ["out"], [12]]]
    NS = len(STAGES)
    WARM_UP = [("x", c) for c in range(CK)] + [("w", c) for c in range(2 * CK)] + \
        [s for s in STAGES if s[0] in "qk"] + [("w", c) for c in range(2 * CK, 3 * CK)] + \
        [s for s in STAGES if s[0] == "v"] + [("w", c) for c in range(3 * CK, 4 * CK)]

    with ExitStack() as ctx:
        def sb(name, shape, dt=FP32):
            return ctx.enter_context(nc.sbuf_tensor(name, shape, dt))

        def ps(name):
            return ctx.enter_context(nc.psum_tensor(name, [P, 512], FP32))

        def sem(name):
            return ctx.enter_context(nc.semaphore(name))

        ident = sb("ident", [P, P])
        w_nat = sb("w_nat", [P, 4, CK, C])
        w_hi = sb("w_hi", [P, 4, CK, C], FP32R)
        w_lo = sb("w_lo", [P, 4, CK, C], FP32R)
        bv_row = sb("bv_row", [P, C])
        bo_row = sb("bo_row", [P, C])
        x_sb = [sb(f"x_sb{n}", [P, QUAD, C]) for n in range(2)]
        adj_sb = [sb(f"adj_sb{n}", [P, QUAD, N]) for n in range(2)]
        adj2 = [sb(f"adj2_{n}", [P, QUAD, N]) for n in range(2)]
        xb = [sb(f"xb{n}", [P, QUAD, C]) for n in range(2)]
        xT_hi = sb("xT_hi", [P, CK, TOK], FP32R)
        xT_lo = sb("xT_lo", [P, CK, TOK], FP32R)
        qT = [sb(f"qT{n}", [P, CK, TOK]) for n in range(2)]
        kT = [sb(f"kT{n}", [P, CK, TOK]) for n in range(2)]
        v_sb = [sb(f"v_sb{n}", [P, QUAD, HEADS, DV]) for n in range(2)]
        neg_scores = [sb(f"neg_scores{n}", [P, HEADS, N]) for n in range(2)]
        probs = [sb(f"probs{n}", [P, HEADS, N]) for n in range(2)]
        probsT = [sb(f"probsT{n}", [P, HB, N]) for n in range(2)]
        neg_max = [sb(f"neg_max{n}", [P, HEADS]) for n in range(2)]
        neg_min = sb("neg_min", [P, HEADS])
        extent = [sb(f"extent{n}", [P, HEADS]) for n in range(2)]
        recip = sb("recip", [P, HEADS])
        weight = sb("weight", [P, HEADS])
        o_sb = sb("o_sb", [P, C])
        oT_hi = sb("oT_hi", [P, CK, N], FP32R)
        oT_lo = sb("oT_lo", [P, CK, N], FP32R)
        z_sb = [sb(f"z_sb{n}", [P, C]) for n in range(2)]
        bn = sb("bn", [P, 6])
        mean_var = [sb(f"mean_var{n}", [P, 2]) for n in range(2)]
        minus_half = sb("minus_half", [P, 1])
        var_eps = sb("var_eps", [P, 1])
        rstd = sb("rstd", [P, 1])
        shift = sb("shift", [P, 1])
        y_out = [sb(f"y_out{n}", [P, C]) for n in range(2)]

        ps_scores = [ps(f"ps_scores{n}") for n in range(2)]
        ps_probsT = [ps(f"ps_probsT{n}") for n in range(2)]
        ps_proj = [ps(f"ps_proj{n}") for n in range(2)]
        ps_o = ps("ps_o")
        ps_y = ps("ps_y")

        w_loaded = [sem(f"w_loaded{n}") for n in range(4)]
        b_loaded = sem("b_loaded")
        x_loaded = [sem(f"x_loaded{n}") for n in range(2)]
        adj_loaded = [sem(f"adj_loaded{n}") for n in range(2)]
        stored = [sem(f"stored{n}") for n in range(2)]
        consts_set = sem("consts_set")
        w_turned = sem("w_turned")
        w_high = sem("w_high")
        w_split = sem("w_split")
        x_turned = sem("x_turned")
        x_high = sem("x_high")
        x_split = sem("x_split")
        qk_ready = sem("qk_ready")
        qk_done = sem("qk_done")
        v_ready = sem("v_ready")
        v_done = sem("v_done")
        adj_doubled = sem("adj_doubled")
        xb_done = sem("xb_done")
        scores_ready = sem("scores_ready")
        biased = sem("biased")
        probs_done = sem("probs_done")
        p_turned = sem("p_turned")
        pT_done = sem("pT_done")
        o_ready = sem("o_ready")
        min_done = sem("min_done")
        extent_done = sem("extent_done")
        recip_done = sem("recip_done")
        weight_done = sem("weight_done")
        o_done = sem("o_done")
        o_turned = sem("o_turned")
        o_high = sem("o_high")
        o_split = sem("o_split")
        y_ready = sem("y_ready")
        z_done = sem("z_done")
        bn_done = sem("bn_done")
        stats_done = sem("stats_done")
        eps_done = sem("eps_done")
        rstd_done = sem("rstd_done")
        shift_done = sem("shift_done")
        passed = sem("passed")
        normed = sem("normed")

        block = ctx.enter_context(nc.Block())

        def some(n):
            return not isinstance(n, int) or n > 0

        def stand(eng):
            eng.sem_inc(passed, 1)

        banks = [*ps_proj, *ps_scores, *ps_probsT, ps_o, ps_y]

        def stage_done(k, q):
            return left_bank(*STAGES[k], q) if k >= 0 else left_bank(*STAGES[k + NS], q - 1)

        def left_bank(kind, c, q):
            if kind == "w":
                return w_split, c + 1
            if kind == "x":
                return x_split, 3 * q + c + 1
            if kind == "v":
                return v_done, QUAD * q + c + 1
            return qk_done, 6 * q + 2 * c + (2 if kind == "k" else 1)

        def bank_of(k, parity):
            return ps_proj[(NS * parity + k) % 2]

        def run(eng, slot, tail):
            def pair(i, first, last):
                for parity in range(2):
                    q = 2 * i + parity
                    for g in range(QUAD):
                        j = parity * QUAD + g
                        slot(2 * QUAD * i + j, g, q, parity, True, not first or j >= 1, not first or j >= 2,
                             not last or parity == 0, not last)

            pair(0, True, False)
            with eng.Fori(1, PAIRS - 1) as i:
                pair(i, False, False)
            pair(PAIRS - 1, False, True)
            if tail:
                slot(GRAPHS, 0, QUADS, 0, False, True, True, False, False)
                slot(GRAPHS + 1, 1, QUADS, 0, False, False, True, False, False)

        @block.sync
        def _(sp):
            def load(q, parity):
                sp.dma_start(x_sb[parity][:, :, :], x_quads[q]).then_inc(x_loaded[parity], 16)
                sp.dma_start(adj_sb[parity][:, :, :], adj_quads[q]).then_inc(adj_loaded[parity], 16)

            load(0, 0)
            weights = [w.rearrange("(t p) c -> p t c", p=P) for w in (wq, wk, wv, wo)]
            for n in range(2):
                sp.dma_start(w_nat[:, n, :, :], weights[n]).then_inc(w_loaded[n], 16)
            for row, b in ((bv_row, bv), (bo_row, bo)):
                sp.dma_start(row[:, :], b.rearrange("(a c) -> a c", a=1).to_broadcast([P, C])).then_inc(b_loaded, 16)
            for n in range(2, 4):
                sp.dma_start(w_nat[:, n, :, :], weights[n]).then_inc(w_loaded[n], 16)
            load(1, 1)

            def slot(G, g, Q, parity, new, old, older, ahead, ahead2):
                if g == 0 and ahead2:
                    sp.wait_ge(x_turned, CK * (Q + 1))
                    stand(sp)
                    sp.wait_ge(xb_done, QUAD * (Q + 1))
                    stand(sp)
                    sp.wait_ge(adj_doubled, Q + 1)
                    stand(sp)
                    load(Q + 2, parity)
                if older:
                    sp.wait_ge(normed, G - 1)
                    stand(sp)
                    sp.dma_start(out[G - 2], y_out[g % 2][:, :]).then_inc(stored[g % 2], 16)

            run(sp, slot, True)
            for n in range(2):
                sp.wait_ge(stored[n], 16 * GRAPHS // 2)

        @block.gpsimd
        def _(pool):
            pool.memset(ident[:, :], 0.0).then_inc(consts_set, 1)
            pool.wait_ge(consts_set, 1)
            pool.affine_select(out=ident[:, :], in_=ident[:, :], compare_op=ALU.not_equal, fill=1.0, base=0,
                               pattern=[[-1, P]], channel_multiplier=1).then_inc(consts_set, 1)
            pool.memset(minus_half[:, :], -0.5).then_inc(consts_set, 1)
            for n in range(2):
                pool.memset(v_sb[n][:, :, :, D:DV], 1.0).then_inc(consts_set, 1)
            pool.wait_ge(consts_set, 5)
            pool.wait_ge(b_loaded, 32)

            def double_adj(q, parity, loads):
                pool.wait_ge(adj_loaded[parity], 16 * loads)
                if some(RG * QUAD * (q - 1)):
                    pool.wait_ge(biased, RG * QUAD * (q - 1))
                pool.tensor_tensor(adj2[parity][:, :, :], adj_sb[parity][:, :, :], adj_sb[parity][:, :, :],
                                   ALU.add).then_inc(adj_doubled, 1)

            def add_bo(G, g, parity, loads):
                pool.wait_ge(x_loaded[parity], 16 * loads)
                if some(G - 2 * QUAD + 1):
                    pool.wait_ge(z_done, G - 2 * QUAD + 1)
                pool.tensor_tensor(xb[parity][:, g, :], x_sb[parity][:, g, :], bo_row[:, :],
                                   ALU.add).then_inc(xb_done, 1)

            double_adj(0, 0, 1)
            for g in range(QUAD):
                add_bo(g, g, 0, 1)

            def normalise(G, n, stores):
                pool.wait_ge(stats_done, G + 1)
                stand(pool)
                pool.tensor_scalar(var_eps[:, :], mean_var[n][:, 1:2], 1.0, EPS, ALU.mult, ALU.add)\
                    .then_inc(eps_done, 1)
                pool.wait_ge(eps_done, G + 1)
                pool.tensor_tensor(rstd[:, :], var_eps[:, :], minus_half[:, :], ALU.pow).then_inc(rstd_done, 1)
                pool.wait_ge(rstd_done, G + 1)
                stand(pool)
                pool.tensor_scalar(shift[:, :], mean_var[n][:, 0:1], -1.0, rstd[:, 0:1], ALU.mult, ALU.mult)\
                    .then_inc(shift_done, 1)
                pool.wait_ge(shift_done, G + 1)
                if some(16 * stores):
                    pool.wait_ge(stored[n], 16 * stores)
                stand(pool)
                pool.tensor_scalar(y_out[n][:, :], z_sb[n][:, :], rstd[:, 0:1], shift[:, 0:1], ALU.mult, ALU.add)\
                    .then_inc(normed, 1)

            def slot(G, g, Q, parity, new, old, older, ahead, ahead2):
                nxt = 1 - parity
                if ahead:
                    loads = (Q - parity) // 2 + parity + 1
                    if g == 0:
                        double_adj(Q + 1, nxt, loads)
                    add_bo(G + QUAD, g, nxt, loads)
                if older:
                    normalise(G - 2, g % 2, stores_before(G, parity, g))

            def stores_before(G, parity, g):
                return (G - 2 - g % 2) // 2

            run(pool, slot, True)

        @block.tensor
        def _(pe):
            pe.wait_ge(consts_set, 5)
            def three_pass(dst, lhs_hi, lhs_lo, rhs_hi, rhs_lo):
                for c in range(CK):
                    pe.matmul(dst, lhs_hi(c), rhs_hi(c), start=(c == 0), stop=False)
                    pe.matmul(dst, lhs_lo(c), rhs_hi(c), start=False, stop=False)
                    mm = pe.matmul(dst, lhs_hi(c), rhs_lo(c), start=False, stop=(c == CK - 1))
                return mm

            def stage(kind, c, bank, q, parity, loads):
                if kind == "w":
                    n, part = c // CK, c % CK
                    pe.wait_ge(w_loaded[n], 16)
                    for t in range(CK):
                        mm = pe.transpose(bank[:, t * P:(t + 1) * P], w_nat[:, n, t, part * P:(part + 1) * P],
                                          ident[:, :])
                    mm.then_inc(w_turned, 1)
                elif kind == "x":
                    if c == 0:
                        pe.wait_ge(x_loaded[parity], 16 * loads)
                    for g in range(QUAD):
                        mm = pe.transpose(bank[:, g * N:(g + 1) * N], x_sb[parity][:, g, c * P:(c + 1) * P],
                                          ident[:, :])
                    mm.then_inc(x_turned, 1)
                elif kind == "v":
                    if isinstance(q, int) and q == 0:
                        pe.wait_ge(w_split, 3 * CK)
                    pe.wait_ge(x_split, CK * (q + 1))
                    tok = slice(c * N, (c + 1) * N)
                    three_pass(bank[:, 0:C], lambda i: xT_hi[:, i, tok], lambda i: xT_lo[:, i, tok],
                               lambda i: w_hi[:, 2, i, :], lambda i: w_lo[:, 2, i, :]).then_inc(v_ready, 1)
                else:
                    n = 0 if kind == "q" else 1
                    col = slice(c * P, (c + 1) * P)
                    if isinstance(q, int) and q == 0:
                        pe.wait_ge(w_split, 2 * CK)
                    pe.wait_ge(x_split, CK * (q + 1))
                    three_pass(bank[:, :], lambda i: w_hi[:, n, i, col], lambda i: w_lo[:, n, i, col],
                               lambda i: xT_hi[:, i, :], lambda i: xT_lo[:, i, :]).then_inc(qk_ready, 1)

            def scores(G, g, Q, parity, b):
                if g == 0 and b == 0:
                    pe.wait_ge(qk_done, 6 * (Q + 1))
                if some(RG * G + b - 1):
                    pe.wait_ge(biased, RG * G + b - 1)
                tok = slice(g * N, (g + 1) * N)
                rows = slice(b * D, (b + 1) * D)
                for i in range(HB):
                    mm = pe.matmul(ps_scores[b % 2][:, i * N:(i + 1) * N], qT[parity][rows, i, tok],
                                   kT[parity][rows, i, tok], start=True, stop=True)
                mm.then_inc(scores_ready, 1)

            def turn_probs(G, n, b):
                pe.wait_ge(probs_done, RG * G + b + 1)
                if some(RG * G + b - 1):
                    pe.wait_ge(pT_done, RG * G + b - 1)
                for i in range(HB):
                    mm = pe.transpose(ps_probsT[b % 2][:, i * N:(i + 1) * N], probs[n][:, b * HB + i, :], ident[:, :])
                mm.then_inc(p_turned, 1)

            def probs_times_v(G, g, parity, b):
                if b == 0:
                    pe.wait_ge(v_done, G + 1)
                    if some(G):
                        pe.wait_ge(o_done, G)
                pe.wait_ge(pT_done, RG * G + b + 1)
                for i in range(HB):
                    h = b + RG * i
                    mm = pe.matmul(ps_o[:, h * DV:(h + 1) * DV], probsT[b % 2][:, i, :], v_sb[parity][:, g, h, :],
                                   start=True, stop=True)
                if b == RG - 1:
                    mm.then_inc(o_ready, 1)

            def turn_heads(G):
                pe.wait_ge(o_done, G + 1)
                if some(G):
                    pe.wait_ge(z_done, G)
                for c in range(CK):
                    mm = pe.transpose(ps_y[:, c * N:(c + 1) * N], o_sb[:, c * P:(c + 1) * P], ident[:, :])
                mm.then_inc(o_turned, 1)

            def project_out(G):
                pe.wait_ge(o_split, G + 1)
                three_pass(ps_y[:, 0:C], lambda i: oT_hi[:, i, :], lambda i: oT_lo[:, i, :],
                           lambda i: w_hi[:, 3, i, :], lambda i: w_lo[:, 3, i, :]).then_inc(y_ready, 1)

            for u, (kind, c) in enumerate(WARM_UP):
                if u >= len(banks):
                    pe.wait_ge(*left_bank(*WARM_UP[u - len(banks)], 0))
                stage(kind, c, banks[u % len(banks)], 0, 0, 1)
            for u in range(len(WARM_UP) - len(banks), len(WARM_UP)):
                pe.wait_ge(*left_bank(*WARM_UP[u], 0))

            def slot(G, g, Q, parity, new, old, older, ahead, ahead2):
                was = (g - 1) % QUAD
                was_parity = parity if g else 1 - parity
                for b in range(RG):
                    if old:
                        turn_probs(G - 1, (g - 1) % 2, b)
                    if new:
                        scores(G, g, Q, parity, b)
                    for k in FILL[g][b]:
                        if k == "turn" and older:
                            turn_heads(G - 2)
                        elif k == "out" and older:
                            project_out(G - 2)
                        elif isinstance(k, int) and ahead:
                            pe.wait_ge(*stage_done(k - 2, Q + 1))
                            stage(*STAGES[k], bank_of(k, 1 - parity), Q + 1, 1 - parity,
                                  (Q - parity) // 2 + parity + 1 if k == 0 else None)
                    if old:
                        probs_times_v(G - 1, was, was_parity, b)

            run(pe, slot, True)

        @block.scalar
        def _(act):
            def stage(kind, c, bank, q, parity):
                if kind == "w":
                    act.wait_ge(w_turned, c + 1)
                    act.activation(w_hi[:, c // CK, c % CK, :], bank[:, 0:C], ACT.Copy).then_inc(w_high, 1)
                elif kind == "x":
                    act.wait_ge(x_turned, CK * q + c + 1)
                    act.activation(xT_hi[:, c, :], bank[:, :], ACT.Copy).then_inc(x_high, 1)
                elif kind in ("q", "k"):
                    act.wait_ge(qk_ready, 6 * q + 2 * c + (2 if kind == "k" else 1))
                    dst = (qT if kind == "q" else kT)[parity]
                    act.activation(dst[:, c, :], bank[:, :], ACT.Copy, scale=SCALE if kind == "q" else 1.0)\
                        .then_inc(qk_done, 1)

            for u, (kind, c) in enumerate(WARM_UP):
                stage(kind, c, banks[u % len(banks)], 0, 0)

            def fill(k, G, Q, parity, older, ahead):
                if k == "turn" and older:
                    act.wait_ge(o_turned, G - 1)
                    act.activation(oT_hi[:, :, :].rearrange("p c n -> p (c n)"), ps_y[:, 0:C], ACT.Copy)\
                        .then_inc(o_high, 1)
                elif isinstance(k, int) and ahead:
                    stage(*STAGES[k], bank_of(k, 1 - parity), Q + 1, 1 - parity)

            def slot(G, g, Q, parity, new, old, older, ahead, ahead2):
                for b in range(RG):
                    if old:
                        act.wait_ge(p_turned, RG * (G - 1) + b + 1)
                        act.activation(probsT[b % 2][:, :, :].rearrange("p i n -> p (i n)"),
                                       ps_probsT[b % 2][:, 0:HB * N], ACT.Copy).then_inc(pT_done, 1)
                    short = [k for k in FILL[g][b] if k == "turn" or isinstance(k, int) and STAGES[k][0] == "x"]
                    for k in short:
                        fill(k, G, Q, parity, older, ahead)
                    if new:
                        act.wait_ge(biased, RG * G + b + 1)
                        for i in range(HB):
                            s = b * HB + i
                            ex = act.activation(probs[g % 2][:, s, :], neg_scores[g % 2][:, s, :], ACT.Exp,
                                                bias=neg_max[g % 2][:, s:s + 1], scale=-1.0)
                        ex.then_inc(probs_done, 1)
                    for k in FILL[g][b]:
                        if k not in short:
                            fill(k, G, Q, parity, older, ahead)

            run(act, slot, True)

        @block.vector
        def _(dve):
            def stage(kind, c, bank, q, parity):
                if kind == "w":
                    n, part = c // CK, c % CK
                    dve.wait_ge(w_high, c + 1)
                    dve.tensor_tensor(w_lo[:, n, part, :], bank[:, 0:C], w_hi[:, n, part, :].bitcast(FP32),
                                      ALU.subtract).then_inc(w_split, 1)
                elif kind == "x":
                    dve.wait_ge(x_high, CK * q + c + 1)
                    dve.tensor_tensor(xT_lo[:, c, :], bank[:, :], xT_hi[:, c, :].bitcast(FP32), ALU.subtract)\
                        .then_inc(x_split, 1)
                elif kind == "v":
                    dve.wait_ge(v_ready, QUAD * q + c + 1)
                    dve.tensor_tensor(v_sb[parity][:, c, :, 0:D], bank[:, 0:C].rearrange("p (h d) -> p h d", d=D),
                                      bv_row[:, :].rearrange("p (h d) -> p h d", d=D), ALU.add).then_inc(v_done, 1)

            dve.wait_ge(b_loaded, 32)
            dve.wait_ge(consts_set, 5)
            for u, (kind, c) in enumerate(WARM_UP):
                stage(kind, c, banks[u % len(banks)], 0, 0)

            def add_bias(G, g, Q, parity, b):
                if g == 0 and b == 0:
                    dve.wait_ge(adj_doubled, Q + 1)
                if b == 0:
                    if some(RG * (G - 1)):
                        dve.wait_ge(probs_done, RG * (G - 1))
                dve.wait_ge(scores_ready, RG * G + b + 1)
                stand(dve)
                for i in range(HB):
                    s = b * HB + i
                    op = dve.tensor_tensor_reduce(neg_scores[g % 2][:, s, :], ps_scores[b % 2][:, i * N:(i + 1) * N],
                                                  adj2[parity][:, g, :], -1.0, NEG_INIT, ALU.add, ALU.min,
                                                  neg_max[g % 2][:, s:s + 1])
                op.then_inc(biased, 1)

            def find_zero_rows(G, n, half):
                heads = slice(half * HEADS // 2, (half + 1) * HEADS // 2)
                dve.wait_ge(biased, RG * (G + 1))
                dve.tensor_reduce(neg_min[:, heads], neg_scores[n][:, heads, :], AX.X, ALU.max).then_inc(min_done, 1)
                dve.wait_ge(min_done, 2 * G + half + 1)
                dve.scalar_tensor_tensor(extent[n][:, heads], neg_max[n][:, heads], -1.0, neg_min[:, heads],
                                         ALU.mult, ALU.max).then_inc(extent_done, 1)

            def normalise_heads(G, n):
                dve.wait_ge(o_ready, G + 1)
                o_view = ps_o[:, 0:HEADS * DV].rearrange("p (h e) -> p h e", e=DV)
                dve.reciprocal(recip[:, :], o_view[:, :, D]).then_inc(recip_done, 1)
                dve.wait_ge(recip_done, G + 1)
                dve.wait_ge(extent_done, 2 * (G + 1))
                dve.scalar_tensor_tensor(weight[:, :].rearrange("p (i b) -> p i b", b=RG),
                                         extent[n][:, :].rearrange("p (b i) -> p i b", i=HB), 0.0,
                                         recip[:, :].rearrange("p (i b) -> p i b", b=RG), ALU.not_equal, ALU.mult)\
                    .then_inc(weight_done, 1)
                dve.wait_ge(weight_done, G + 1)
                if some(G):
                    dve.wait_ge(o_turned, G)
                dve.tensor_tensor(o_sb[:, :].rearrange("p (h d) -> p h d", d=D), o_view[:, :, 0:D],
                                  weight[:, :].rearrange("p (h a) -> p h a", a=1).to_broadcast([P, HEADS, D]),
                                  ALU.mult).then_inc(o_done, 1)

            def split_heads(G):
                dve.wait_ge(o_high, G + 1)
                dve.tensor_tensor(oT_lo[:, :, :].rearrange("p c n -> p (c n)"), ps_y[:, 0:C],
                                  oT_hi[:, :, :].rearrange("p c n -> p (c n)").bitcast(FP32),
                                  ALU.subtract).then_inc(o_split, 1)

            def residual(G, g, parity, n):
                dve.wait_ge(y_ready, G + 1)
                dve.wait_ge(xb_done, G + 1)
                if some(G - 1):
                    dve.wait_ge(normed, G - 1)
                dve.tensor_tensor(z_sb[n][:, :], ps_y[:, 0:C], xb[parity][:, g, :], ALU.add).then_inc(z_done, 1)
                dve.wait_ge(z_done, G + 1)
                dve.bn_stats(bn[:, :], z_sb[n][:, :]).then_inc(bn_done, 1)
                dve.wait_ge(bn_done, G + 1)
                stand(dve)
                dve.bn_aggr(mean_var[n][:, :], bn[:, :]).then_inc(stats_done, 1)

            def slot(G, g, Q, parity, new, old, older, ahead, ahead2):
                for b in range(RG):
                    if new:
                        add_bias(G, g, Q, parity, b)
                    for k in FILL[g][b]:
                        if k == "turn" and older:
                            split_heads(G - 2)
                        elif k == "out" and older:
                            residual(G - 2, (g - 2) % QUAD, parity if g >= 2 else 1 - parity, g % 2)
                        elif isinstance(k, int) and ahead:
                            stage(*STAGES[k], bank_of(k, 1 - parity), Q + 1, 1 - parity)
                    if old and b < 2:
                        find_zero_rows(G - 1, (g - 1) % 2, b)
                if old:
                    normalise_heads(G - 1, (g - 1) % 2)

            run(dve, slot, True)


_INS = ["x", "adj", "L0_gnn_Wq", "L0_gnn_Wk", "L0_gnn_Wv", "L0_gnn_bv", "L0_gnn_Wo", "L0_gnn_bo"]
_OUTS = [((64, 128, 384), "float32")]


def kernel(**inputs):
    import numpy as _np
    import concourse.bacc as _bacc
    from concourse import mybir as _mybir
    from concourse.bass_utils import run_bass_kernel_spmd as _run

    nc = _bacc.Bacc("TRN2", target_bir_lowering=False, num_devices=1)
    arrays, args = {}, []
    for name in _INS:
        a = _np.ascontiguousarray(inputs[name])
        arrays[f"in_{name}_dram"] = a
        args.append(nc.dram_tensor(f"in_{name}_dram", a.shape, _mybir.dt.from_np(a.dtype), kind="ExternalInput").ap())
    for i, (shape, dtype) in enumerate(_OUTS):
        dt = _mybir.dt.from_np(_np.dtype(dtype))
        args.append(nc.dram_tensor(f"out_{i}_dram", shape, dt, kind="ExternalOutput").ap())
    graph_attention_layernorm(nc, *args)
    r = _run(nc, [arrays], core_ids=[0])
    return r.results[0]["out_0_dram"]
```

```python
from contextlib import ExitStack

import concourse.bass as bass
from concourse import mybir

FP32 = mybir.dt.float32
FP32R = mybir.dt.float32r
ALU = mybir.AluOpType
ACT = mybir.ActivationFunctionType
AX = mybir.AxisListType


def graph_attention_layernorm(nc, x, adj, wq, wk, wv, bv, wo, bo, out):
    GRAPHS, N, C = x.shape
    HEADS = 12
    D = C // HEADS
    P = 128
    CK = C // P
    QUAD = 4
    TOK = QUAD * N
    QUADS = GRAPHS // QUAD
    PAIRS = QUADS // 2
    RG = P // D
    HB = HEADS // RG
    DV = D + 1
    SCALE = float(C) ** -0.5
    EPS = 1e-5
    NEG_INIT = 3.0e38

    x_quads = x.rearrange("(q g) p c -> q p g c", g=QUAD)
    adj_quads = adj.rearrange("(q g) p k -> q p g k", g=QUAD)

    STAGES = [("x", 0), ("x", 1), ("x", 2), ("q", 0), ("k", 0), ("q", 1), ("k", 1), ("q", 2), ("k", 2),
              ("v", 0), ("v", 1), ("v", 2), ("v", 3)]
    FILL = [[[0, 1, "turn", "pv"], [2], ["out", "pv"], ["pv", 3, "pv"]],
            [[4, "pv"], ["turn", 5, "pv"], ["out", "pv"], [6, "pv"]],
            [[7, "pv"], ["turn", 8, "pv"], ["out", "pv"], [9, "pv"]],
            [[10, "pv"], ["turn", 11, "pv"], ["out", "pv"], [12, "pv"]]]
    DRAIN = [[[], ["turn", "pv"], ["pv"], ["out", "pv", "pv"]]] * QUAD
    NS = len(STAGES)
    WARM_UP = ["x0", "x1", "x2", "w0", "w1", "w2", "w3", "w4", "w5", "q0", "w6", "k0", "w7", "q1", "w8", "k1",
               "w9", "q2", "w10", "k2", "w11", "v0", "v1", "v2", "v3"]
    WARM_UP = [(s[0], int(s[1:])) for s in WARM_UP]

    with ExitStack() as ctx:
        def sb(name, shape, dt=FP32):
            return ctx.enter_context(nc.sbuf_tensor(name, shape, dt))

        def ps(name):
            return ctx.enter_context(nc.psum_tensor(name, [P, 512], FP32))

        def sem(name):
            return ctx.enter_context(nc.semaphore(name))

        ident = sb("ident", [P, P])
        w_hi = sb("w_hi", [P, 4, CK, C], FP32R)
        w_lo = sb("w_lo", [P, 4, CK, C], FP32R)
        bv_row = sb("bv_row", [P, C])
        bo_row = sb("bo_row", [P, C])
        x_sb = [sb(f"x_sb{n}", [P, QUAD, C]) for n in range(2)]
        adj_sb = [sb(f"adj_sb{n}", [P, QUAD, N]) for n in range(2)]
        adj2 = [sb(f"adj2_{n}", [P, QUAD, N]) for n in range(2)]
        xb = [sb(f"xb{n}", [P, QUAD, C]) for n in range(2)]
        xT_hi = sb("xT_hi", [P, CK, TOK], FP32R)
        xT_lo = sb("xT_lo", [P, CK, TOK], FP32R)
        q_hi, q_lo, k_hi, k_lo = ([sb(f"{name}{n}", [P, QUAD, CK, N], FP32R) for n in range(2)]
                                  for name in ("q_hi", "q_lo", "k_hi", "k_lo"))
        q_stack = [sb(f"q_stack{n}", [3 * D, RG, CK, N], FP32R) for n in range(2)]
        k_stack = [sb(f"k_stack{n}", [3 * D, RG, CK, N], FP32R) for n in range(2)]
        v_sb = [sb(f"v_sb{n}", [P, QUAD, HEADS, DV]) for n in range(2)]
        neg_scores = [sb(f"neg_scores{n}", [P, HEADS, N]) for n in range(2)]
        probs = [sb(f"probs{n}", [P, HEADS, N]) for n in range(2)]
        probsT = [sb(f"probsT{n}", [P, HB, N]) for n in range(2)]
        w_nat = [t[:, 0:CK * C // N, :].rearrange("p a b -> p (a b)").rearrange("p (t c) -> p t c", c=C)
                 for t in (*neg_scores, *probs)]
        neg_max = [sb(f"neg_max{n}", [P, HEADS]) for n in range(2)]
        neg_min = sb("neg_min", [P, HEADS])
        extent = [sb(f"extent{n}", [P, HEADS]) for n in range(2)]
        recip = sb("recip", [P, HEADS])
        weight = sb("weight", [P, HEADS])
        o_sb = sb("o_sb", [P, C])
        oT_hi = sb("oT_hi", [P, CK, N], FP32R)
        oT_lo = sb("oT_lo", [P, CK, N], FP32R)
        z_sb = [sb(f"z_sb{n}", [P, C]) for n in range(2)]
        bn = sb("bn", [P, 6])
        mean_var = [sb(f"mean_var{n}", [P, 2]) for n in range(2)]
        minus_half = sb("minus_half", [P, 1])
        var_eps = sb("var_eps", [P, 1])
        rstd = sb("rstd", [P, 1])
        shift = sb("shift", [P, 1])
        y_out = [sb(f"y_out{n}", [P, C]) for n in range(2)]

        ps_scores = [ps(f"ps_scores{n}") for n in range(2)]
        ps_probsT = [ps(f"ps_probsT{n}") for n in range(2)]
        ps_proj = [ps(f"ps_proj{n}") for n in range(2)]
        ps_o = ps("ps_o")
        ps_y = ps("ps_y")

        w_loaded = [sem(f"w_loaded{n}") for n in range(4)]
        b_loaded = sem("b_loaded")
        x_loaded = [sem(f"x_loaded{n}") for n in range(2)]
        adj_loaded = [sem(f"adj_loaded{n}") for n in range(2)]
        stored = [sem(f"stored{n}") for n in range(2)]
        consts_set = sem("consts_set")
        w_turned = sem("w_turned")
        w_high = sem("w_high")
        w_split = sem("w_split")
        x_turned = sem("x_turned")
        x_high = sem("x_high")
        x_split = sem("x_split")
        qk_ready = sem("qk_ready")
        qk_high = sem("qk_high")
        qk_split = sem("qk_split")
        stacked = [sem(f"stacked{n}") for n in range(2)]
        v_ready = sem("v_ready")
        v_done = sem("v_done")
        adj_doubled = sem("adj_doubled")
        xb_done = sem("xb_done")
        scores_ready = sem("scores_ready")
        biased = sem("biased")
        probs_done = sem("probs_done")
        p_turned = sem("p_turned")
        pT_done = sem("pT_done")
        o_ready = sem("o_ready")
        min_done = sem("min_done")
        extent_done = sem("extent_done")
        recip_done = sem("recip_done")
        weight_done = sem("weight_done")
        o_done = sem("o_done")
        o_turned = sem("o_turned")
        o_high = sem("o_high")
        o_split = sem("o_split")
        y_ready = sem("y_ready")
        z_done = sem("z_done")
        bn_done = sem("bn_done")
        stats_done = sem("stats_done")
        eps_done = sem("eps_done")
        rstd_done = sem("rstd_done")
        shift_done = sem("shift_done")
        passed = sem("passed")
        normed = sem("normed")

        block = ctx.enter_context(nc.Block())

        def w_columns(w, c):
            w = w[:, c // CK, c % CK, :]
            return w.rearrange("p (t d j) -> p t d j", d=D, j=RG) if c < 2 * CK else w

        def bank_columns(bank, c):
            bank = bank[:, 0:C]
            return bank.rearrange("p (t j d) -> p t d j", d=D, j=RG) if c < 2 * CK else bank

        def some(n):
            return not isinstance(n, int) or n > 0

        def stand(eng):
            eng.sem_inc(passed, 1)

        banks = [ps_proj[0], *ps_scores, *ps_probsT, ps_o, ps_y, ps_proj[1]]

        def stage_done(k, q):
            return left_bank(*STAGES[k], q) if k >= 0 else left_bank(*STAGES[k + NS], q - 1)

        def left_bank(kind, c, q):
            if kind == "w":
                return w_split, c + 1
            if kind == "x":
                return x_split, 3 * q + c + 1
            if kind == "v":
                return v_done, QUAD * q + c + 1
            return qk_split, 6 * q + 2 * c + (2 if kind == "k" else 1)

        def bank_of(k, parity):
            return ps_proj[(NS * parity + k) % 2]

        def steps(g, b, ahead):
            return (FILL if ahead else DRAIN)[g][b]

        def run(eng, slot, tail):
            def pair(i, first, last):
                for parity in range(2):
                    q = 2 * i + parity
                    for g in range(QUAD):
                        j = parity * QUAD + g
                        slot(2 * QUAD * i + j, g, q, parity, True, not first or j >= 1, not first or j >= 2,
                             not last or parity == 0, not last)

            pair(0, True, False)
            with eng.Fori(1, PAIRS - 1) as i:
                pair(i, False, False)
            pair(PAIRS - 1, False, True)
            if tail:
                slot(GRAPHS, 0, QUADS, 0, False, True, True, False, False)
                slot(GRAPHS + 1, 1, QUADS, 0, False, False, True, False, False)

        @block.sync
        def _(sp):
            def load_x(q, parity):
                sp.dma_start(x_sb[parity][:, :, :], x_quads[q]).then_inc(x_loaded[parity], 16)

            def load_adj(q, parity):
                sp.dma_start(adj_sb[parity][:, :, :], adj_quads[q]).then_inc(adj_loaded[parity], 16)

            load_x(0, 0)
            weights = [w.rearrange("(t p) c -> p t c", p=P) for w in (wq, wk, wv, wo)]
            for n in range(4):
                sp.dma_start(w_nat[n], weights[n]).then_inc(w_loaded[n], 16)
            for row, b in ((bv_row, bv), (bo_row, bo)):
                sp.dma_start(row[:, :], b.rearrange("(a c) -> a c", a=1).to_broadcast([P, C])).then_inc(b_loaded, 16)
            load_adj(0, 0)
            load_x(1, 1)
            load_adj(1, 1)

            def stack(dst, parts, g, parity):
                for r, part in enumerate(parts):
                    sp.dma_start(dst[g % 2][r * D:(r + 1) * D, :, :, :].bitcast(FP32),
                                 part[parity][:, g, :, :].bitcast(FP32)).then_inc(stacked[g % 2], 16)

            sp.wait_ge(qk_split, 2 * CK - 1)
            stack(q_stack, (q_hi, q_lo, q_hi), 0, 0)
            sp.wait_ge(qk_split, 2 * CK)
            stack(k_stack, (k_hi, k_hi, k_lo), 0, 0)

            def slot(G, g, Q, parity, new, old, older, ahead, ahead2):
                if new and (not isinstance(G, int) or G + 1 < GRAPHS):
                    if some(RG * G):
                        sp.wait_ge(scores_ready, RG * G)
                        stand(sp)
                    if g == QUAD - 1:
                        sp.wait_ge(qk_split, 6 * (Q + 2))
                        stand(sp)
                    nxt, nxt_parity = (g + 1) % QUAD, parity if g < QUAD - 1 else 1 - parity
                    stack(q_stack, (q_hi, q_lo, q_hi), nxt, nxt_parity)
                    stack(k_stack, (k_hi, k_hi, k_lo), nxt, nxt_parity)
                if g == 0 and ahead2:
                    sp.wait_ge(x_turned, CK * (Q + 1))
                    stand(sp)
                    sp.wait_ge(xb_done, QUAD * (Q + 1))
                    stand(sp)
                    sp.wait_ge(adj_doubled, Q + 1)
                    stand(sp)
                    load_x(Q + 2, parity)
                    load_adj(Q + 2, parity)
                if not isinstance(G, int) or G >= 3:
                    sp.wait_ge(normed, G - 2)
                    stand(sp)
                    sp.dma_start(out[G - 3], y_out[(g + 1) % 2][:, :]).then_inc(stored[(g + 1) % 2], 16)

            run(sp, slot, True)
            sp.wait_ge(normed, GRAPHS)
            sp.dma_start(out[GRAPHS - 1], y_out[(GRAPHS - 1) % 2][:, :]).then_inc(stored[(GRAPHS - 1) % 2], 16)
            for n in range(2):
                sp.wait_ge(stored[n], 16 * GRAPHS // 2)

        @block.gpsimd
        def _(pool):
            pool.memset(ident[:, :], 0.0).then_inc(consts_set, 1)
            pool.wait_ge(consts_set, 1)
            pool.affine_select(out=ident[:, :], in_=ident[:, :], compare_op=ALU.not_equal, fill=1.0, base=0,
                               pattern=[[-1, P]], channel_multiplier=1).then_inc(consts_set, 1)
            pool.memset(minus_half[:, :], -0.5).then_inc(consts_set, 1)
            for n in range(2):
                pool.memset(v_sb[n][:, :, :, D:DV], 1.0).then_inc(consts_set, 1)
            pool.wait_ge(consts_set, 5)
            pool.wait_ge(b_loaded, 32)

            def double_adj(q, parity, loads):
                pool.wait_ge(adj_loaded[parity], 16 * loads)
                if some(RG * QUAD * (q - 1)):
                    pool.wait_ge(biased, RG * QUAD * (q - 1))
                pool.tensor_tensor(adj2[parity][:, :, :], adj_sb[parity][:, :, :], adj_sb[parity][:, :, :],
                                   ALU.add).then_inc(adj_doubled, 1)

            def add_bo(G, g, parity, loads):
                pool.wait_ge(x_loaded[parity], 16 * loads)
                if some(G - 2 * QUAD + 1):
                    pool.wait_ge(z_done, G - 2 * QUAD + 1)
                pool.tensor_tensor(xb[parity][:, g, :], x_sb[parity][:, g, :], bo_row[:, :],
                                   ALU.add).then_inc(xb_done, 1)

            double_adj(0, 0, 1)
            for g in range(QUAD):
                add_bo(g, g, 0, 1)

            def normalise(G, n, stores):
                pool.wait_ge(stats_done, G + 1)
                stand(pool)
                pool.tensor_scalar(var_eps[:, :], mean_var[n][:, 1:2], 1.0, EPS, ALU.mult, ALU.add)\
                    .then_inc(eps_done, 1)
                pool.wait_ge(eps_done, G + 1)
                pool.tensor_tensor(rstd[:, :], var_eps[:, :], minus_half[:, :], ALU.pow).then_inc(rstd_done, 1)
                pool.wait_ge(rstd_done, G + 1)
                stand(pool)
                pool.tensor_scalar(shift[:, :], mean_var[n][:, 0:1], -1.0, rstd[:, 0:1], ALU.mult, ALU.mult)\
                    .then_inc(shift_done, 1)
                pool.wait_ge(shift_done, G + 1)
                if some(16 * stores):
                    pool.wait_ge(stored[n], 16 * stores)
                stand(pool)
                pool.tensor_scalar(y_out[n][:, :], z_sb[n][:, :], rstd[:, 0:1], shift[:, 0:1], ALU.mult, ALU.add)\
                    .then_inc(normed, 1)

            def slot(G, g, Q, parity, new, old, older, ahead, ahead2):
                nxt = 1 - parity
                if ahead:
                    loads = (Q - parity) // 2 + parity + 1
                    if g == 0:
                        double_adj(Q + 1, nxt, loads)
                    add_bo(G + QUAD, g, nxt, loads)
                if older:
                    normalise(G - 2, g % 2, stores_before(G, parity, g))

            def stores_before(G, parity, g):
                return (G - 2 - g % 2) // 2

            run(pool, slot, True)

        @block.tensor
        def _(pe):
            pe.wait_ge(consts_set, 5)
            def three_pass(dst, lhs_hi, lhs_lo, rhs_hi, rhs_lo):
                for c in range(CK):
                    pe.matmul(dst, lhs_hi(c), rhs_hi(c), start=(c == 0), stop=False)
                    pe.matmul(dst, lhs_lo(c), rhs_hi(c), start=False, stop=False)
                    mm = pe.matmul(dst, lhs_hi(c), rhs_lo(c), start=False, stop=(c == CK - 1))
                return mm

            def stage(kind, c, bank, q, parity, loads):
                if kind == "w":
                    n, part = c // CK, c % CK
                    pe.wait_ge(w_loaded[n], 16)
                    for t in range(CK):
                        mm = pe.transpose(bank[:, t * P:(t + 1) * P], w_nat[n][:, t, part * P:(part + 1) * P],
                                          ident[:, :])
                    mm.then_inc(w_turned, 1)
                elif kind == "x":
                    if c == 0:
                        pe.wait_ge(x_loaded[parity], 16 * loads)
                    for g in range(QUAD):
                        mm = pe.transpose(bank[:, g * N:(g + 1) * N], x_sb[parity][:, g, c * P:(c + 1) * P],
                                          ident[:, :])
                    mm.then_inc(x_turned, 1)
                elif kind == "v":
                    if isinstance(q, int) and q == 0:
                        pe.wait_ge(w_split, 3 * CK)
                    pe.wait_ge(x_split, CK * (q + 1))
                    tok = slice(c * N, (c + 1) * N)
                    three_pass(bank[:, 0:C], lambda i: xT_hi[:, i, tok], lambda i: xT_lo[:, i, tok],
                               lambda i: w_hi[:, 2, i, :], lambda i: w_lo[:, 2, i, :]).then_inc(v_ready, 1)
                else:
                    n = 0 if kind == "q" else 1
                    col = slice(c * P, (c + 1) * P)
                    if isinstance(q, int) and q == 0:
                        pe.wait_ge(w_split, (n + 1) * CK)
                    pe.wait_ge(x_split, CK * (q + 1))
                    three_pass(bank[:, :], lambda i: w_hi[:, n, i, col], lambda i: w_lo[:, n, i, col],
                               lambda i: xT_hi[:, i, :], lambda i: xT_lo[:, i, :]).then_inc(qk_ready, 1)

            def scores(G, g, b, before):
                if b == 0:
                    pe.wait_ge(stacked[g % 2], 6 * 16 * (before + 1))
                if some(RG * G + b - 1):
                    pe.wait_ge(biased, RG * G + b - 1)
                for i in range(HB):
                    mm = pe.matmul(ps_scores[b % 2][:, i * N:(i + 1) * N], q_stack[g % 2][:, b, i, :],
                                   k_stack[g % 2][:, b, i, :], start=True, stop=True)
                mm.then_inc(scores_ready, 1)

            def turn_probs(G, n, b):
                pe.wait_ge(probs_done, RG * G + b + 1)
                if some(RG * G + b - 1):
                    pe.wait_ge(pT_done, RG * G + b - 1)
                for i in range(HB):
                    mm = pe.transpose(ps_probsT[b % 2][:, i * N:(i + 1) * N], probs[n][:, b * HB + i, :], ident[:, :])
                mm.then_inc(p_turned, 1)

            def probs_times_v(G, g, parity, b):
                if b == 0:
                    pe.wait_ge(v_done, G + 1)
                    if some(G):
                        pe.wait_ge(o_done, G)
                pe.wait_ge(pT_done, RG * G + b + 1)
                for i in range(HB):
                    h = b + RG * i
                    mm = pe.matmul(ps_o[:, h * DV:(h + 1) * DV], probsT[b % 2][:, i, :], v_sb[parity][:, g, h, :],
                                   start=True, stop=True)
                if b == RG - 1:
                    mm.then_inc(o_ready, 1)

            def turn_heads(G):
                pe.wait_ge(o_done, G + 1)
                if some(G):
                    pe.wait_ge(z_done, G)
                for c in range(CK):
                    mm = pe.transpose(ps_y[:, c * N:(c + 1) * N], o_sb[:, c * P:(c + 1) * P], ident[:, :])
                mm.then_inc(o_turned, 1)

            def project_out(G):
                pe.wait_ge(o_split, G + 1)
                three_pass(ps_y[:, 0:C], lambda i: oT_hi[:, i, :], lambda i: oT_lo[:, i, :],
                           lambda i: w_hi[:, 3, i, :], lambda i: w_lo[:, 3, i, :]).then_inc(y_ready, 1)

            for u, (kind, c) in enumerate(WARM_UP):
                if u >= len(banks):
                    pe.wait_ge(*left_bank(*WARM_UP[u - len(banks)], 0))
                stage(kind, c, banks[u % len(banks)], 0, 0, 1)
            for u in range(len(WARM_UP) - len(banks), len(WARM_UP) - 2):
                pe.wait_ge(*left_bank(*WARM_UP[u], 0))

            def slot(G, g, Q, parity, new, old, older, ahead, ahead2):
                multiplied = 0
                for b in range(RG):
                    if old:
                        turn_probs(G - 1, (g - 1) % 2, b)
                    if new:
                        scores(G, g, b, (G - g % 2) // 2)
                    for k in steps(g, b, ahead):
                        if k == "pv" and old:
                            probs_times_v(G - 1, (g - 1) % QUAD, parity if g else 1 - parity, multiplied)
                            multiplied += 1
                        elif k == "turn" and older:
                            turn_heads(G - 2)
                        elif k == "out" and older:
                            project_out(G - 2)
                        elif isinstance(k, int) and ahead:
                            pe.wait_ge(*stage_done(k - 2, Q + 1))
                            stage(*STAGES[k], bank_of(k, 1 - parity), Q + 1, 1 - parity,
                                  (Q - parity) // 2 + parity + 1 if k == 0 else None)

            run(pe, slot, True)

        @block.scalar
        def _(act):
            def stage(kind, c, bank, q, parity):
                if kind == "w":
                    act.wait_ge(w_turned, c + 1)
                    act.activation(w_columns(w_hi, c), bank_columns(bank, c), ACT.Copy).then_inc(w_high, 1)
                elif kind == "x":
                    act.wait_ge(x_turned, CK * q + c + 1)
                    act.activation(xT_hi[:, c, :], bank[:, :], ACT.Copy).then_inc(x_high, 1)
                elif kind in ("q", "k"):
                    act.wait_ge(qk_ready, 6 * q + 2 * c + (2 if kind == "k" else 1))
                    dst = (q_hi if kind == "q" else k_hi)[parity]
                    act.activation(dst[:, :, c, :], bank[:, :].rearrange("p (g n) -> p g n", n=N), ACT.Copy,
                                   scale=SCALE if kind == "q" else 1.0).then_inc(qk_high, 1)

            for u, (kind, c) in enumerate(WARM_UP):
                stage(kind, c, banks[u % len(banks)], 0, 0)

            def fill(k, G, Q, parity, older, ahead):
                if k == "turn" and older:
                    act.wait_ge(o_turned, G - 1)
                    act.activation(oT_hi[:, :, :].rearrange("p c n -> p (c n)"), ps_y[:, 0:C], ACT.Copy)\
                        .then_inc(o_high, 1)
                elif isinstance(k, int) and ahead:
                    stage(*STAGES[k], bank_of(k, 1 - parity), Q + 1, 1 - parity)

            def exponentials(G, n, b):
                act.wait_ge(biased, RG * G + b + 1)
                for i in range(HB):
                    s = b * HB + i
                    ex = act.activation(probs[n][:, s, :], neg_scores[n][:, s, :], ACT.Exp,
                                        bias=neg_max[n][:, s:s + 1], scale=-1.0)
                ex.then_inc(probs_done, 1)

            def slot(G, g, Q, parity, new, old, older, ahead, ahead2):
                for b in range(RG):
                    if old:
                        act.wait_ge(p_turned, RG * (G - 1) + b + 1)
                        act.activation(probsT[b % 2][:, :, :].rearrange("p i n -> p (i n)"),
                                       ps_probsT[b % 2][:, 0:HB * N], ACT.Copy).then_inc(pT_done, 1)
                    if b and new:
                        exponentials(G, g % 2, b - 1)
                    elif b == 0 and old:
                        exponentials(G - 1, (g - 1) % 2, RG - 1)
                    for k in steps(g, b, ahead):
                        fill(k, G, Q, parity, older, ahead)

            run(act, slot, True)

        @block.vector
        def _(dve):
            def stage(kind, c, bank, q, parity):
                if kind == "w":
                    dve.wait_ge(w_high, c + 1)
                    dve.tensor_tensor(w_columns(w_lo, c), bank_columns(bank, c), w_columns(w_hi, c).bitcast(FP32),
                                      ALU.subtract).then_inc(w_split, 1)
                elif kind == "x":
                    dve.wait_ge(x_high, CK * q + c + 1)
                    dve.tensor_tensor(xT_lo[:, c, :], bank[:, :], xT_hi[:, c, :].bitcast(FP32), ALU.subtract)\
                        .then_inc(x_split, 1)
                elif kind in ("q", "k"):
                    hi, lo = (q_hi, q_lo) if kind == "q" else (k_hi, k_lo)
                    dve.wait_ge(qk_high, 6 * q + 2 * c + (2 if kind == "k" else 1))
                    dve.scalar_tensor_tensor(lo[parity][:, :, c, :], bank[:, :].rearrange("p (g n) -> p g n", n=N),
                                             SCALE if kind == "q" else 1.0, hi[parity][:, :, c, :].bitcast(FP32),
                                             ALU.mult, ALU.subtract).then_inc(qk_split, 1)
                elif kind == "v":
                    if isinstance(q, int) and q == 0 and c == 0:
                        dve.wait_ge(b_loaded, 32)
                    dve.wait_ge(v_ready, QUAD * q + c + 1)
                    dve.tensor_tensor(v_sb[parity][:, c, :, 0:D], bank[:, 0:C].rearrange("p (h d) -> p h d", d=D),
                                      bv_row[:, :].rearrange("p (h d) -> p h d", d=D), ALU.add).then_inc(v_done, 1)

            for u, (kind, c) in enumerate(WARM_UP):
                stage(kind, c, banks[u % len(banks)], 0, 0)

            def add_bias(G, g, Q, parity, b):
                if g == 0 and b == 0:
                    dve.wait_ge(adj_doubled, Q + 1)
                if b == 0:
                    if some(RG * (G - 1)):
                        dve.wait_ge(probs_done, RG * (G - 1))
                dve.wait_ge(scores_ready, RG * G + b + 1)
                stand(dve)
                for i in range(HB):
                    s = b * HB + i
                    op = dve.tensor_tensor_reduce(neg_scores[g % 2][:, s, :], ps_scores[b % 2][:, i * N:(i + 1) * N],
                                                  adj2[parity][:, g, :], -1.0, NEG_INIT, ALU.add, ALU.min,
                                                  neg_max[g % 2][:, s:s + 1])
                op.then_inc(biased, 1)

            def find_zero_rows(G, n, half):
                heads = slice(half * HEADS // 2, (half + 1) * HEADS // 2)
                dve.wait_ge(biased, RG * (G + 1))
                dve.tensor_reduce(neg_min[:, heads], neg_scores[n][:, heads, :], AX.X, ALU.max).then_inc(min_done, 1)
                dve.wait_ge(min_done, 2 * G + half + 1)
                dve.scalar_tensor_tensor(extent[n][:, heads], neg_max[n][:, heads], -1.0, neg_min[:, heads],
                                         ALU.mult, ALU.max).then_inc(extent_done, 1)

            def normalise_heads(G, n):
                dve.wait_ge(o_ready, G + 1)
                o_view = ps_o[:, 0:HEADS * DV].rearrange("p (h e) -> p h e", e=DV)
                dve.reciprocal(recip[:, :], o_view[:, :, D]).then_inc(recip_done, 1)
                dve.wait_ge(recip_done, G + 1)
                dve.wait_ge(extent_done, 2 * (G + 1))
                dve.scalar_tensor_tensor(weight[:, :].rearrange("p (i b) -> p i b", b=RG),
                                         extent[n][:, :].rearrange("p (b i) -> p i b", i=HB), 0.0,
                                         recip[:, :].rearrange("p (i b) -> p i b", b=RG), ALU.not_equal, ALU.mult)\
                    .then_inc(weight_done, 1)
                dve.wait_ge(weight_done, G + 1)
                if some(G):
                    dve.wait_ge(o_turned, G)
                dve.tensor_tensor(o_sb[:, :].rearrange("p (h d) -> p h d", d=D), o_view[:, :, 0:D],
                                  weight[:, :].rearrange("p (h a) -> p h a", a=1).to_broadcast([P, HEADS, D]),
                                  ALU.mult).then_inc(o_done, 1)

            def split_heads(G):
                dve.wait_ge(o_high, G + 1)
                dve.tensor_tensor(oT_lo[:, :, :].rearrange("p c n -> p (c n)"), ps_y[:, 0:C],
                                  oT_hi[:, :, :].rearrange("p c n -> p (c n)").bitcast(FP32),
                                  ALU.subtract).then_inc(o_split, 1)

            def residual(G, g, parity, n):
                dve.wait_ge(y_ready, G + 1)
                dve.wait_ge(xb_done, G + 1)
                if some(G - 1):
                    dve.wait_ge(normed, G - 1)
                dve.tensor_tensor(z_sb[n][:, :], ps_y[:, 0:C], xb[parity][:, g, :], ALU.add).then_inc(z_done, 1)
                dve.wait_ge(z_done, G + 1)
                dve.bn_stats(bn[:, :], z_sb[n][:, :]).then_inc(bn_done, 1)
                dve.wait_ge(bn_done, G + 1)
                stand(dve)
                dve.bn_aggr(mean_var[n][:, :], bn[:, :]).then_inc(stats_done, 1)

            def slot(G, g, Q, parity, new, old, older, ahead, ahead2):
                for b in range(RG):
                    if new:
                        add_bias(G, g, Q, parity, b)
                    for k in steps(g, b, ahead):
                        if k == "turn" and older:
                            split_heads(G - 2)
                        elif k == "out" and older:
                            residual(G - 2, (g - 2) % QUAD, parity if g >= 2 else 1 - parity, g % 2)
                        elif isinstance(k, int) and ahead and STAGES[k][0] not in "qk":
                            stage(*STAGES[k], bank_of(k, 1 - parity), Q + 1, 1 - parity)
                    late = steps(g, b - 1, ahead) if b else steps(g - 1, RG - 1, ahead) if g else []
                    for k in late:
                        if isinstance(k, int) and ahead and STAGES[k][0] in "qk":
                            stage(*STAGES[k], bank_of(k, 1 - parity), Q + 1, 1 - parity)
                    if old and b < 2:
                        find_zero_rows(G - 1, (g - 1) % 2, b)
                if old:
                    normalise_heads(G - 1, (g - 1) % 2)

            run(dve, slot, True)


_INS = ["x", "adj", "L0_gnn_Wq", "L0_gnn_Wk", "L0_gnn_Wv", "L0_gnn_bv", "L0_gnn_Wo", "L0_gnn_bo"]
_OUTS = [((64, 128, 384), "float32")]


def kernel(**inputs):
    import numpy as _np
    import concourse.bacc as _bacc
    from concourse import mybir as _mybir
    from concourse.bass_utils import run_bass_kernel_spmd as _run

    nc = _bacc.Bacc("TRN2", target_bir_lowering=False, num_devices=1)
    arrays, args = {}, []
    for name in _INS:
        a = _np.ascontiguousarray(inputs[name])
        arrays[f"in_{name}_dram"] = a
        args.append(nc.dram_tensor(f"in_{name}_dram", a.shape, _mybir.dt.from_np(a.dtype), kind="ExternalInput").ap())
    for i, (shape, dtype) in enumerate(_OUTS):
        dt = _mybir.dt.from_np(_np.dtype(dtype))
        args.append(nc.dram_tensor(f"out_{i}_dram", shape, dt, kind="ExternalOutput").ap())
    graph_attention_layernorm(nc, *args)
    r = _run(nc, [arrays], core_ids=[0])
    return r.results[0]["out_0_dram"]
```
